# Optimizing a Trainium2 kernel written in Bass

```python
import numpy as np
import jax
import jax.numpy as jnp

def _softmax(x, axis=-1):
    return jax.nn.softmax(x, axis=axis)

def _gelu(x):
    return jax.nn.gelu(x, approximate=True)

def _silu(x):
    return jax.nn.silu(x)

def _sigmoid(x):
    return jax.nn.sigmoid(x)

def _layernorm(x, axis=-1, eps=1e-05):
    m = jnp.mean(x, axis=axis, keepdims=True)
    v = jnp.var(x, axis=axis, keepdims=True)
    return (x - m) / jnp.sqrt(v + eps)

def _scatter_add(tgt, idx, src, axis=0):
    return tgt.at[idx].add(src)

def _segment_sum(src, seg, n):
    return jax.ops.segment_sum(src, seg, n)
kernel_name = 'mk_rec_standalone_d1_rec_r8_58e040'

def setup_inputs(seed: int=0):
    np.random.seed(seed)
    _w = jnp.asarray

    def _rec_inputs():
        import jax
        import jax.numpy as jnp
        _rk = jax.random.key(seed)
        r_inputs_A = -0.000292821 + 1.00034 * jax.random.normal(jax.random.fold_in(_rk, 1), (2048, 32, 64), jnp.float32)
        r_inputs_B = -1.39393e-06 + 0.999914 * jax.random.normal(jax.random.fold_in(_rk, 2), (2048, 32, 64), jnp.float32)
        return (r_inputs_A, r_inputs_B)
    r_inputs_A, r_inputs_B = _rec_inputs()

    def _L0_rec_setup():
        import jax, jax.numpy as jnp
        import numpy as np
        BATCH, F, E = (256, 32, 64)
        key = jax.random.key(seed)
        kA, kB, kW = jax.random.split(key, 3)
        inputs_A = jax.random.normal(kA, (BATCH, F, E), dtype=jnp.float32)
        inputs_B = jax.random.normal(kB, (BATCH, F, E), dtype=jnp.float32)
        W = jax.random.normal(kW, (F, E, E), dtype=jnp.float32) * (1.0 / np.sqrt(E))
        return {'inputs_A': inputs_A, 'inputs_B': inputs_B, 'W': W}
    _L0_rec_all = _L0_rec_setup()
    _L0_rec_in = {k: v for k, v in _L0_rec_all.items() if k in ('W',)}
    del _L0_rec_all
    return {'r_inputs_A': r_inputs_A, 'r_inputs_B': r_inputs_B, 'L0_rec_W': _L0_rec_in['W']}

def reference(r_inputs_A, r_inputs_B, L0_rec_W):
    import jax
    import jax.numpy as jnp

    def _L0_rec_ref(inputs_A, inputs_B, W):
        import jax, jax.numpy as jnp
        import numpy as np
        BATCH, F, E = (256, 32, 64)
        proj = jnp.einsum('bfe,fde->bfd', inputs_A, W)
        B_, F_, E_ = inputs_A.shape
        p = proj[:, :, None, :] * inputs_B[:, None, :, :]
        return p.reshape(B_, F_ * F_, E_)
    y = _L0_rec_ref(r_inputs_A, r_inputs_B, L0_rec_W)
    return y

_drawn_inputs = setup_inputs


def setup_inputs(seed=0):
    import zlib

    import numpy as np

    out = dict(_drawn_inputs(seed))
    spreads = {}
    factors = {}
    for name, (base, spread) in spreads.items():
        noise = np.random.default_rng([zlib.crc32(name.encode()), seed]).standard_normal(out[name].shape)
        drawn = base * np.exp(spread * noise) if base else spread * noise
        out[name] = jnp.asarray(drawn.astype(out[name].dtype))
    for name, factor in factors.items():
        out[name] = (out[name] * factor).astype(out[name].dtype)
    return out
```

```python
import concourse.bass as bass
from concourse import mybir
from contextlib import ExitStack


def bass_field_pair_products(nc: bass.Bass, A: bass.AP, B: bass.AP, W: bass.AP, out: bass.AP):
    fp32 = mybir.dt.float32
    ALU = mybir.AluOpType

    P = 128
    BATCH, F, E = A.shape
    FE = F * E
    BLOCKS = BATCH // P
    IN_SLOTS = 2
    TRIPS = BLOCKS // IN_SLOTS

    PAIR = P // E
    PAIRS = F // PAIR
    GROUP = 4
    GROUPS = PAIRS // GROUP
    PROJ_SLOTS = 2 * GROUPS
    OUT_SLOTS = 8
    CHUNK = PAIR * FE

    a_dram = A.rearrange("(n p) f e -> n p (f e)", p=P)
    b_dram = B.rearrange("(n p) f e -> n p (f e)", p=P)
    w_dram = W.rearrange("(q s) d e -> s d q e", s=PAIR)
    out_dram = out.rearrange("(n p) (c r) e -> n c p (r e)", p=P, c=PAIRS)

    with ExitStack() as ctx:
        def sb(name, shape):
            return ctx.enter_context(nc.sbuf_tensor(name, shape, fp32))

        def pb(name, shape):
            return ctx.enter_context(nc.psum_tensor(name, shape, fp32))

        def sem(name):
            return ctx.enter_context(nc.semaphore(name))

        ident = sb("ident", [P, P])
        w_diag = sb("w_diag", [P, PAIRS, P])
        w_t = sb("w_t", [P, PAIRS, P])
        a_in = sb("a_in", [P, IN_SLOTS, FE])
        b_in = sb("b_in", [P, IN_SLOTS, FE])
        a_t = sb("a_t", [P, 2, GROUP * P])
        proj = sb("proj", [P, PROJ_SLOTS, GROUP * P])
        products = sb("products", [P, OUT_SLOTS, CHUNK])

        t_psum = [pb(f"t_psum{i}", [P, GROUP * P]) for i in range(2)]
        w_psum = [pb(f"w_psum{i}", [P, GROUP * P]) for i in range(2)]
        p_psum = [pb(f"p_psum{i}", [P, GROUP * P]) for i in range(2)]

        ident_zeroed = sem("ident_zeroed")
        ident_ready = sem("ident_ready")
        w_zeroed = sem("w_zeroed")
        w_first_loaded = sem("w_first_loaded")
        w_rest_loaded = sem("w_rest_loaded")
        a_first_loaded = sem("a_first_loaded")
        a_loaded = [sem(f"a_loaded{s}") for s in range(IN_SLOTS)]
        b_loaded = [sem(f"b_loaded{s}") for s in range(IN_SLOTS)]
        w_transposed = sem("w_transposed")
        w_copied = sem("w_copied")
        a_transposed = sem("a_transposed")
        a_copied = sem("a_copied")
        projected = sem("projected")
        proj_copied = sem("proj_copied")
        multiplied = sem("multiplied")
        stored = [sem(f"stored{s}") for s in range(OUT_SLOTS)]

        block = ctx.enter_context(nc.Block())

        @block.gpsimd
        def _(pool):
            nc.gpsimd.memset(ident[:], 0.0).then_inc(ident_zeroed, 1)
            pool.wait_ge(ident_zeroed, 1)
            nc.gpsimd.affine_select(out=ident[:], in_=ident[:], compare_op=ALU.not_equal, fill=1.0, base=0,
                                    pattern=[[-1, P]], channel_multiplier=1).then_inc(ident_ready, 1)

        @block.sync
        def _(sp):
            def load_a(n, s):
                sp.dma_start(a_in[:, s, :], a_dram[n, :, :]).then_inc(a_loaded[s], 16)

            def load_b(n, s):
                sp.dma_start(b_in[:, s, :], b_dram[n, :, :]).then_inc(b_loaded[s], 16)

            def trip(t, prefetch):
                for s in range(IN_SLOTS):
                    n = t * IN_SLOTS + s
                    for c in range(PAIRS):
                        sp.wait_ge(multiplied, n * PAIRS + (c + 1))
                        sp.dma_start(out_dram[n, c, :, :],
                                     products[:, c % OUT_SLOTS, :]).then_inc(stored[c % OUT_SLOTS], 16)
                    if prefetch:
                        sp.wait_ge(a_transposed, n * GROUPS + GROUPS)
                        load_a(n + IN_SLOTS, s)
                        load_b(n + IN_SLOTS, s)

            g0 = GROUP * P
            sp.dma_start(a_in[:, 0, 0:g0], a_dram[0, :, 0:g0]).then_inc(a_first_loaded, 16)
            load_b(0, 0)
            sp.dma_start(a_in[:, 0, g0:FE], a_dram[0, :, g0:FE]).then_inc(a_loaded[0], 16)
            for s in range(1, IN_SLOTS):
                load_a(s, s)
                load_b(s, s)
            with sp.Fori(0, TRIPS - 1) as t:
                trip(t, True)
            trip(TRIPS - 1, False)
            for s in range(OUT_SLOTS):
                sp.wait_ge(stored[s], 16 * (BLOCKS * PAIRS // OUT_SLOTS))

        @block.scalar
        def _(act):
            for lo, hi, loaded in ((0, GROUP, w_first_loaded), (GROUP, PAIRS, w_rest_loaded)):
                for s in range(PAIR):
                    act.dma_start(w_diag[s * E:(s + 1) * E, lo:hi, s * E:(s + 1) * E],
                                  w_dram[s, :, lo:hi, :]).then_inc(loaded, 16)

            def group(k, g, s, first):
                if first:
                    act.wait_ge(w_transposed, g + 1)
                    nc.scalar.copy(w_t[:, g * GROUP:(g + 1) * GROUP, :].rearrange("p q m -> p (q m)"),
                                   w_psum[g % 2][:]).then_inc(w_copied, 1)
                act.wait_ge(a_transposed, k + 1)
                if not first or g >= 2:
                    act.wait_ge(projected, k - 1)
                nc.scalar.copy(a_t[:, g % 2, :], t_psum[g % 2][:]).then_inc(a_copied, 1)
                act.wait_ge(projected, k + 1)
                if not first and not (isinstance(k, int) and k < PROJ_SLOTS):
                    act.wait_ge(multiplied, (k + 1 - PROJ_SLOTS) * GROUP)
                nc.scalar.copy(proj[:, s * GROUPS + g, :], p_psum[g % 2][:]).then_inc(proj_copied, 1)

            def trip(t, first_trip):
                for s in range(IN_SLOTS):
                    for g in range(GROUPS):
                        group((t * IN_SLOTS + s) * GROUPS + g, g, s, first_trip and s == 0)

            trip(0, True)
            with act.Fori(1, TRIPS) as t:
                trip(t, False)

        @block.tensor
        def _(pe):
            def group(k, g, s, first):
                if first:
                    if g < 2:
                        pe.wait_ge((w_first_loaded, w_rest_loaded)[g], 16 * PAIR)
                    else:
                        pe.wait_ge(w_copied, g - 1)
                    for q in range(GROUP):
                        last = nc.tensor.transpose(w_psum[g % 2][:, q * P:(q + 1) * P],
                                                   w_diag[:, g * GROUP + q, :], ident[:])
                    last.then_inc(w_transposed, 1)
                    if g < 2:
                        pe.wait_ge((a_first_loaded, a_loaded[0])[g], 16)
                if not first or g >= 2:
                    pe.wait_ge(a_copied, k - 1)
                for q in range(GROUP):
                    col = (g * GROUP + q) * P
                    last = nc.tensor.transpose(t_psum[g % 2][:, q * P:(q + 1) * P],
                                               a_in[:, s, col:col + P], ident[:])
                last.then_inc(a_transposed, 1)
                if first:
                    pe.wait_ge(w_copied, g + 1)
                pe.wait_ge(a_copied, k + 1)
                if not first or g >= 2:
                    pe.wait_ge(proj_copied, k - 1)
                for q in range(GROUP):
                    last = nc.tensor.matmul(p_psum[g % 2][:, q * P:(q + 1) * P], a_t[:, g % 2, q * P:(q + 1) * P],
                                            w_t[:, g * GROUP + q, :], start=True, stop=True)
                last.then_inc(projected, 1)

            def trip(t, first_trip):
                for s in range(IN_SLOTS):
                    if not (first_trip and s == 0):
                        pe.wait_ge(a_loaded[s], t * 16 + 16)
                    for g in range(GROUPS):
                        group((t * IN_SLOTS + s) * GROUPS + g, g, s, first_trip and s == 0)

            pe.wait_ge(ident_ready, 1)
            pe.wait_ge(w_zeroed, 2)
            trip(0, True)
            with pe.Fori(1, TRIPS) as t:
                trip(t, False)

        @block.vector
        def _(dve):
            def trip(t, first_trip):
                for s in range(IN_SLOTS):
                    n = t * IN_SLOTS + s
                    dve.wait_ge(b_loaded[s], t * 16 + 16)
                    b_all = b_in[:, s, :].rearrange("p (r f e) -> p r f e", r=1, e=E).to_broadcast([P, PAIR, F, E])
                    for c in range(PAIRS):
                        g, q = c // GROUP, c % GROUP
                        if q == 0:
                            dve.wait_ge(proj_copied, n * GROUPS + (g + 1))
                        if not (first_trip and s == 0 and c < OUT_SLOTS):
                            dve.wait_ge(stored[c % OUT_SLOTS],
                                        16 * (n * (PAIRS // OUT_SLOTS) + c // OUT_SLOTS))
                        p_pair = proj[:, s * GROUPS + g, q * P:(q + 1) * P].rearrange(
                            "p (r f e) -> p r f e", f=1, e=E).to_broadcast([P, PAIR, F, E])
                        o = products[:, c % OUT_SLOTS, :].rearrange("p (r f e) -> p r f e", f=F, e=E)
                        nc.vector.tensor_tensor(o, p_pair, b_all, ALU.mult).then_inc(multiplied, 1)

            nc.vector.memset(w_diag[0:E, :, E:P], 0.0).then_inc(w_zeroed, 1)
            nc.vector.memset(w_diag[E:P, :, 0:E], 0.0).then_inc(w_zeroed, 1)

            trip(0, True)
            with dve.Fori(1, TRIPS) as t:
                trip(t, False)


_INS = ['r_inputs_A', 'r_inputs_B', 'L0_rec_W']


def kernel(**inputs):
    import numpy as _np
    import concourse.bacc as _bacc
    from concourse import mybir as _mybir
    from concourse.bass_utils import run_bass_kernel_spmd as _run

    nc = _bacc.Bacc("TRN2", target_bir_lowering=False, num_devices=1)
    arrays, args = {}, []
    for name in _INS:
        a = _np.ascontiguousarray(inputs[name])
        arrays[f"in_{name}_dram"] = a
        args.append(nc.dram_tensor(f"in_{name}_dram", a.shape, _mybir.dt.from_np(a.dtype), kind="ExternalInput").ap())
    batch, fields, width = inputs['r_inputs_A'].shape
    args.append(nc.dram_tensor("out_0_dram", (batch, fields * fields, width), _mybir.dt.float32,
                               kind="ExternalOutput").ap())
    bass_field_pair_products(nc, *args)
    r = _run(nc, [arrays], core_ids=[0])
    return r.results[0]["out_0_dram"]
```

```python
import concourse.bass as bass
from concourse import mybir
from contextlib import ExitStack


def bass_field_pair_products(nc: bass.Bass, A: bass.AP, B: bass.AP, W: bass.AP, out: bass.AP):
    fp32 = mybir.dt.float32
    ALU = mybir.AluOpType

    P = 128
    BATCH, F, E = A.shape
    FE = F * E
    BLOCKS = BATCH // P
    IN_SLOTS = 2
    TRIPS = BLOCKS // IN_SLOTS

    PAIR = P // E
    PAIRS = F // PAIR
    BANK = 512
    GROUP = BANK // P
    GROUPS = PAIRS // GROUP
    OUT_SLOTS = 8
    CHUNK = PAIR * FE

    a_dram = A.rearrange("(n p) f e -> n p (f e)", p=P)
    b_dram = B.rearrange("(n p) f e -> n p (f e)", p=P)
    w_dram = W.rearrange("(q s) d e -> s d q e", s=PAIR)
    out_dram = out.rearrange("(n p) (c r) e -> n c p (r e)", p=P, c=PAIRS)

    with ExitStack() as ctx:
        def sb(name, shape):
            return ctx.enter_context(nc.sbuf_tensor(name, shape, fp32))

        def pb(name, shape):
            return ctx.enter_context(nc.psum_tensor(name, shape, fp32))

        def sem(name):
            return ctx.enter_context(nc.semaphore(name))

        ident = sb("ident", [P, P])
        w_diag = sb("w_diag", [P, PAIRS, P])
        w_t = sb("w_t", [P, PAIRS, P])
        a_in = sb("a_in", [P, IN_SLOTS, FE])
        b_in = sb("b_in", [P, IN_SLOTS, FE])
        a_t = sb("a_t", [P, 2, GROUP * P])
        products = sb("products", [P, OUT_SLOTS, CHUNK])

        t_psum = [pb(f"t_psum{i}", [P, GROUP * P]) for i in range(2)]
        w_psum = [pb(f"w_psum{i}", [P, GROUP * P]) for i in range(2)]
        proj = [pb(f"proj{g}", [P, GROUP * P]) for g in range(GROUPS)]

        ident_zeroed = sem("ident_zeroed")
        ident_ready = sem("ident_ready")
        w_zeroed = sem("w_zeroed")
        w_first_loaded = sem("w_first_loaded")
        w_rest_loaded = sem("w_rest_loaded")
        a_first_loaded = sem("a_first_loaded")
        a_loaded = [sem(f"a_loaded{s}") for s in range(IN_SLOTS)]
        b_loaded = [sem(f"b_loaded{s}") for s in range(IN_SLOTS)]
        w_transposed = sem("w_transposed")
        w_copied = sem("w_copied")
        a_transposed = sem("a_transposed")
        a_copied = sem("a_copied")
        projected = sem("projected")
        multiplied = sem("multiplied")
        first_field_multiplied = sem("first_field_multiplied")
        first_field_stored = sem("first_field_stored")
        stored = [sem(f"stored{s}") for s in range(OUT_SLOTS)]

        block = ctx.enter_context(nc.Block())

        @block.gpsimd
        def _(pool):
            nc.gpsimd.memset(ident[:], 0.0).then_inc(ident_zeroed, 1)
            pool.wait_ge(ident_zeroed, 1)
            nc.gpsimd.affine_select(out=ident[:], in_=ident[:], compare_op=ALU.not_equal, fill=1.0, base=0,
                                    pattern=[[-1, P]], channel_multiplier=1).then_inc(ident_ready, 1)

        @block.sync
        def _(sp):
            def load_a(n, s):
                sp.dma_start(a_in[:, s, :], a_dram[n, :, :]).then_inc(a_loaded[s], 16)

            def load_b(n, s):
                sp.dma_start(b_in[:, s, :], b_dram[n, :, :]).then_inc(b_loaded[s], 16)

            def trip(t, first_trip, prefetch):
                for s in range(IN_SLOTS):
                    n = t * IN_SLOTS + s
                    for c in range(PAIRS):
                        e0 = 0
                        if first_trip and s == 0 and c == 0:
                            e0 = FE
                            sp.wait_ge(first_field_multiplied, 1)
                            sp.dma_start(out_dram[0, 0, :, 0:e0],
                                         products[:, 0, 0:e0]).then_inc(first_field_stored, 16)
                        sp.wait_ge(multiplied, n * PAIRS + (c + 1))
                        sp.dma_start(out_dram[n, c, :, e0:CHUNK],
                                     products[:, c % OUT_SLOTS, e0:CHUNK]).then_inc(stored[c % OUT_SLOTS], 16)
                    if prefetch:
                        sp.wait_ge(a_transposed, n * GROUPS + GROUPS)
                        load_a(n + IN_SLOTS, s)
                        load_b(n + IN_SLOTS, s)

            def load_w(lo, hi, loaded):
                for h in range(PAIR):
                    sp.dma_start(w_diag[h * E:(h + 1) * E, lo:hi, h * E:(h + 1) * E],
                                 w_dram[h, :, lo:hi, :]).then_inc(loaded, 16)

            g0 = GROUP * P
            load_w(0, GROUP, w_first_loaded)
            sp.dma_start(a_in[:, 0, 0:g0], a_dram[0, :, 0:g0]).then_inc(a_first_loaded, 16)
            load_b(0, 0)
            load_w(GROUP, PAIRS, w_rest_loaded)
            sp.dma_start(a_in[:, 0, g0:FE], a_dram[0, :, g0:FE]).then_inc(a_loaded[0], 16)
            for s in range(1, IN_SLOTS):
                load_a(s, s)
                load_b(s, s)
            trip(0, True, True)
            with sp.Fori(1, TRIPS - 1) as t:
                trip(t, False, True)
            trip(TRIPS - 1, False, False)
            sp.wait_ge(first_field_stored, 16)
            for s in range(OUT_SLOTS):
                sp.wait_ge(stored[s], 16 * (BLOCKS * PAIRS // OUT_SLOTS))

        @block.scalar
        def _(act):
            def group(k, g, first):
                if first:
                    act.wait_ge(w_transposed, g + 1)
                    nc.scalar.copy(w_t[:, g * GROUP:(g + 1) * GROUP, :].rearrange("p q m -> p (q m)"),
                                   w_psum[g % 2][:]).then_inc(w_copied, 1)
                act.wait_ge(a_transposed, k + 1)
                if not first or g >= 2:
                    act.wait_ge(projected, k - 1)
                nc.scalar.copy(a_t[:, g % 2, :], t_psum[g % 2][:]).then_inc(a_copied, 1)

            def trip(t, first_trip):
                for s in range(IN_SLOTS):
                    for g in range(GROUPS):
                        group((t * IN_SLOTS + s) * GROUPS + g, g, first_trip and s == 0)

            trip(0, True)
            with act.Fori(1, TRIPS) as t:
                trip(t, False)

        @block.tensor
        def _(pe):
            def group(k, g, s, first):
                if first:
                    if g < 2:
                        pe.wait_ge((w_first_loaded, w_rest_loaded)[g], 16 * PAIR)
                    else:
                        pe.wait_ge(w_copied, g - 1)
                    for q in range(GROUP):
                        last = nc.tensor.transpose(w_psum[g % 2][:, q * P:(q + 1) * P],
                                                   w_diag[:, g * GROUP + q, :], ident[:])
                    last.then_inc(w_transposed, 1)
                    if g < 2:
                        pe.wait_ge((a_first_loaded, a_loaded[0])[g], 16)
                if not first or g >= 2:
                    pe.wait_ge(a_copied, k - 1)
                for q in range(GROUP):
                    col = (g * GROUP + q) * P
                    last = nc.tensor.transpose(t_psum[g % 2][:, q * P:(q + 1) * P],
                                               a_in[:, s, col:col + P], ident[:])
                last.then_inc(a_transposed, 1)
                if first:
                    pe.wait_ge(w_copied, g + 1)
                pe.wait_ge(a_copied, k + 1)
                if not first:
                    pe.wait_ge(multiplied, (k + 1 - GROUPS) * GROUP)
                for q in range(GROUP):
                    last = nc.tensor.matmul(proj[g][:, q * P:(q + 1) * P], a_t[:, g % 2, q * P:(q + 1) * P],
                                            w_t[:, g * GROUP + q, :], start=True, stop=True)
                last.then_inc(projected, 1)

            def trip(t, first_trip):
                for s in range(IN_SLOTS):
                    if not (first_trip and s == 0):
                        pe.wait_ge(a_loaded[s], t * 16 + 16)
                    for g in range(GROUPS):
                        group((t * IN_SLOTS + s) * GROUPS + g, g, s, first_trip and s == 0)

            pe.wait_ge(ident_ready, 1)
            pe.wait_ge(w_zeroed, 2)
            trip(0, True)
            with pe.Fori(1, TRIPS) as t:
                trip(t, False)

        @block.vector
        def _(dve):
            def trip(t, first_trip):
                for s in range(IN_SLOTS):
                    n = t * IN_SLOTS + s
                    dve.wait_ge(b_loaded[s], t * 16 + 16)
                    b_all = b_in[:, s, :].rearrange("p (r f e) -> p r f e", r=1, e=E).to_broadcast([P, PAIR, F, E])
                    for c in range(PAIRS):
                        g, q = c // GROUP, c % GROUP
                        if q == 0:
                            dve.wait_ge(projected, n * GROUPS + (g + 1))
                        if not (first_trip and s == 0 and c < OUT_SLOTS):
                            dve.wait_ge(stored[c % OUT_SLOTS],
                                        16 * (n * (PAIRS // OUT_SLOTS) + c // OUT_SLOTS))
                            if first_trip and s == 0 and c == OUT_SLOTS:
                                dve.wait_ge(first_field_stored, 16)
                        p_pair = proj[g][:, q * P:(q + 1) * P].rearrange(
                            "p (r f e) -> p r f e", f=1, e=E).to_broadcast([P, PAIR, F, E])
                        o = products[:, c % OUT_SLOTS, :].rearrange("p (r f e) -> p r f e", f=F, e=E)
                        r0 = 0
                        if first_trip and s == 0 and c == 0:
                            r0 = 1
                            nc.vector.tensor_tensor(o[:, 0:r0], p_pair[:, 0:r0], b_all[:, 0:r0],
                                                    ALU.mult).then_inc(first_field_multiplied, 1)
                        nc.vector.tensor_tensor(o[:, r0:PAIR], p_pair[:, r0:PAIR], b_all[:, r0:PAIR],
                                                ALU.mult).then_inc(multiplied, 1)

            nc.vector.memset(w_diag[0:E, :, E:P], 0.0).then_inc(w_zeroed, 1)
            nc.vector.memset(w_diag[E:P, :, 0:E], 0.0).then_inc(w_zeroed, 1)

            trip(0, True)
            with dve.Fori(1, TRIPS) as t:
                trip(t, False)


_INS = ['r_inputs_A', 'r_inputs_B', 'L0_rec_W']


def kernel(**inputs):
    import numpy as _np
    import concourse.bacc as _bacc
    from concourse import mybir as _mybir
    from concourse.bass_utils import run_bass_kernel_spmd as _run

    nc = _bacc.Bacc("TRN2", target_bir_lowering=False, num_devices=1)
    arrays, args = {}, []
    for name in _INS:
        a = _np.ascontiguousarray(inputs[name])
        arrays[f"in_{name}_dram"] = a
        args.append(nc.dram_tensor(f"in_{name}_dram", a.shape, _mybir.dt.from_np(a.dtype), kind="ExternalInput").ap())
    batch, fields, width = inputs['r_inputs_A'].shape
    args.append(nc.dram_tensor("out_0_dram", (batch, fields * fields, width), _mybir.dt.float32,
                               kind="ExternalOutput").ap())
    bass_field_pair_products(nc, *args)
    r = _run(nc, [arrays], core_ids=[0])
    return r.results[0]["out_0_dram"]
```

```python
import concourse.bass as bass
from concourse import mybir
from contextlib import ExitStack


def bass_field_pair_products(nc: bass.Bass, A: bass.AP, B: bass.AP, W: bass.AP, out: bass.AP):
    fp32 = mybir.dt.float32
    ALU = mybir.AluOpType

    P = 128
    BATCH, F, E = A.shape
    FE = F * E
    BLOCKS = BATCH // P
    IN_SLOTS = 2
    TRIPS = BLOCKS // IN_SLOTS

    BANK = 512
    GROUP = BANK // P
    GROUPS = F // GROUP
    PROJ_SLOTS = 4
    W_ROWS = P // GROUP
    D_ROWS = E // W_ROWS
    FIELDS = 2
    CHUNKS = F // FIELDS
    GROUP_CHUNKS = GROUP // FIELDS
    OUT_SLOTS = 8
    CHUNK = FIELDS * FE

    a_dram = A.rearrange("(n p) f e -> n p (f e)", p=P)
    b_dram = B.rearrange("(n p) f e -> n p (f e)", p=P)
    w_dram = W.rearrange("(g s) (h r) e -> (s h) g (r e)", s=GROUP, r=D_ROWS)
    out_dram = out.rearrange("(n p) (c r) e -> n c p (r e)", p=P, c=CHUNKS)

    with ExitStack() as ctx:
        def sb(name, shape):
            return ctx.enter_context(nc.sbuf_tensor(name, shape, fp32))

        def pb(name, shape):
            return ctx.enter_context(nc.psum_tensor(name, shape, fp32))

        def sem(name):
            return ctx.enter_context(nc.semaphore(name))

        ident = sb("ident", [P, P])
        w_in = sb("w_in", [P, GROUPS, D_ROWS * E])
        w_t = sb("w_t", [E, F, E])
        a_in = sb("a_in", [P, IN_SLOTS, FE])
        b_in = sb("b_in", [P, IN_SLOTS, FE])
        a_t = sb("a_t", [E, 2, GROUP * P])
        products = sb("products", [P, OUT_SLOTS, CHUNK])

        w_psum = [pb(f"w_psum{i}", [E, BANK]) for i in range(2)]
        t_psum = [pb(f"t_psum{i}", [E, BANK]) for i in range(2)]
        proj = [pb(f"proj{i}", [P, BANK]) for i in range(PROJ_SLOTS)]

        ident_zeroed = sem("ident_zeroed")
        ident_ready = sem("ident_ready")
        w_first_loaded = sem("w_first_loaded")
        w_rest_loaded = sem("w_rest_loaded")
        a_first_loaded = sem("a_first_loaded")
        b_first_loaded = sem("b_first_loaded")
        a_loaded = [sem(f"a_loaded{s}") for s in range(IN_SLOTS)]
        b_loaded = [sem(f"b_loaded{s}") for s in range(IN_SLOTS)]
        w_transposed = sem("w_transposed")
        w_copied = sem("w_copied")
        a_transposed = sem("a_transposed")
        a_copied = sem("a_copied")
        projected = sem("projected")
        multiplied = sem("multiplied")
        first_field_multiplied = sem("first_field_multiplied")
        first_field_stored = sem("first_field_stored")
        stored = [sem(f"stored{s}") for s in range(OUT_SLOTS)]

        block = ctx.enter_context(nc.Block())

        @block.gpsimd
        def _(pool):
            nc.gpsimd.memset(ident[:], 0.0).then_inc(ident_zeroed, 1)
            pool.wait_ge(ident_zeroed, 1)
            nc.gpsimd.affine_select(out=ident[:], in_=ident[:], compare_op=ALU.not_equal, fill=1.0, base=0,
                                    pattern=[[-1, P]], channel_multiplier=1).then_inc(ident_ready, 1)

        @block.sync
        def _(sp):
            def load_a(n, s):
                sp.dma_start(a_in[:, s, :], a_dram[n, :, :]).then_inc(a_loaded[s], 16)

            def load_b(n, s):
                sp.dma_start(b_in[:, s, :], b_dram[n, :, :]).then_inc(b_loaded[s], 16)

            def trip(t, first_trip, prefetch):
                for s in range(IN_SLOTS):
                    n = t * IN_SLOTS + s
                    for c in range(CHUNKS):
                        e0 = 0
                        if first_trip and s == 0 and c == 0:
                            e0 = FE
                            sp.wait_ge(first_field_multiplied, 1)
                            sp.dma_start(out_dram[0, 0, :, 0:e0],
                                         products[:, 0, 0:e0]).then_inc(first_field_stored, 16)
                        sp.wait_ge(multiplied, n * CHUNKS + (c + 1))
                        sp.dma_start(out_dram[n, c, :, e0:CHUNK],
                                     products[:, c % OUT_SLOTS, e0:CHUNK]).then_inc(stored[c % OUT_SLOTS], 16)
                    if prefetch:
                        sp.wait_ge(a_transposed, n * GROUPS + GROUPS)
                        load_a(n + IN_SLOTS, s)
                        load_b(n + IN_SLOTS, s)

            g0, half = GROUP * E, FE // 2
            sp.dma_start(b_in[:, 0, 0:half], b_dram[0, :, 0:half]).then_inc(b_first_loaded, 16)
            sp.dma_start(w_in[:, 0:1, :], w_dram[:, 0:1, :]).then_inc(w_first_loaded, 16)
            sp.dma_start(a_in[:, 0, 0:g0], a_dram[0, :, 0:g0]).then_inc(a_first_loaded, 16)
            sp.dma_start(b_in[:, 0, half:FE], b_dram[0, :, half:FE]).then_inc(b_loaded[0], 16)
            sp.dma_start(w_in[:, 1:GROUPS, :], w_dram[:, 1:GROUPS, :]).then_inc(w_rest_loaded, 16)
            sp.dma_start(a_in[:, 0, g0:FE], a_dram[0, :, g0:FE]).then_inc(a_loaded[0], 16)
            for s in range(1, IN_SLOTS):
                load_a(s, s)
                load_b(s, s)
            trip(0, True, True)
            with sp.Fori(1, TRIPS - 1) as t:
                trip(t, False, True)
            trip(TRIPS - 1, False, False)
            sp.wait_ge(first_field_stored, 16)
            for s in range(OUT_SLOTS):
                sp.wait_ge(stored[s], 16 * (BLOCKS * CHUNKS // OUT_SLOTS))

        @block.scalar
        def _(act):
            def group(k, g, first):
                if first:
                    act.wait_ge(w_transposed, g + 1)
                    nc.scalar.copy(
                        w_t[:, g * GROUP:(g + 1) * GROUP, :].rearrange("e s (h r) -> e r s h", r=D_ROWS),
                        w_psum[g % 2][:, 0:GROUP * E].rearrange("e (r s h) -> e r s h", r=D_ROWS, s=GROUP),
                    ).then_inc(w_copied, 1)
                act.wait_ge(a_transposed, k + 1)
                if not first or g >= 2:
                    act.wait_ge(projected, k - 1)
                nc.scalar.copy(a_t[:, g % 2, :], t_psum[g % 2][:]).then_inc(a_copied, 1)

            def trip(t, first_trip):
                for s in range(IN_SLOTS):
                    for g in range(GROUPS):
                        group((t * IN_SLOTS + s) * GROUPS + g, g, first_trip and s == 0)

            trip(0, True)
            with act.Fori(1, TRIPS) as t:
                trip(t, False)

        @block.tensor
        def _(pe):

            def transpose_group(k, g, s, first):
                if first:
                    if g < 2:
                        pe.wait_ge((w_first_loaded, w_rest_loaded)[g], 16)
                    else:
                        pe.wait_ge(w_copied, g - 1)
                    for r in range(D_ROWS):
                        last = nc.tensor.transpose(w_psum[g % 2][:, r * P:(r + 1) * P],
                                                   w_in[:, g, r * E:(r + 1) * E], ident[:])
                    last.then_inc(w_transposed, 1)
                    if g < 2:
                        pe.wait_ge((a_first_loaded, a_loaded[0])[g], 16)
                for q in range(GROUP):
                    col = (g * GROUP + q) * E
                    last = nc.tensor.transpose(t_psum[g % 2][:, q * P:(q + 1) * P],
                                               a_in[:, s, col:col + E], ident[:])
                last.then_inc(a_transposed, 1)

            def project_group(k, g, first):
                if first:
                    pe.wait_ge(w_copied, g + 1)
                pe.wait_ge(a_copied, k + 1)
                if not first or g >= PROJ_SLOTS:
                    pe.wait_ge(multiplied, (k + 1 - PROJ_SLOTS) * GROUP_CHUNKS)
                for q in range(GROUP):
                    last = nc.tensor.matmul(proj[g % PROJ_SLOTS][:, q * E:(q + 1) * E],
                                            a_t[:, g % 2, q * P:(q + 1) * P],
                                            w_t[:, g * GROUP + q, :], start=True, stop=True)
                last.then_inc(projected, 1)

            def trip(t, first_trip, last_trip):
                for s in range(IN_SLOTS):
                    for g in range(GROUPS):
                        transpose_group((t * IN_SLOTS + s) * GROUPS + g, g, s, first_trip and s == 0)
                        if g == GROUPS - 1 and not (last_trip and s == IN_SLOTS - 1):
                            pe.wait_ge(a_loaded[(s + 1) % IN_SLOTS], (t + (s + 1) // IN_SLOTS) * 16 + 16)
                        project_group((t * IN_SLOTS + s) * GROUPS + g, g, first_trip and s == 0)

            pe.wait_ge(ident_ready, 1)
            trip(0, True, False)
            with pe.Fori(1, TRIPS - 1) as t:
                trip(t, False, False)
            trip(TRIPS - 1, False, True)

        @block.vector
        def _(dve):
            def trip(t, first_trip):
                for s in range(IN_SLOTS):
                    n = t * IN_SLOTS + s
                    if first_trip and s == 0:
                        dve.wait_ge(b_first_loaded, 16)
                    dve.wait_ge(b_loaded[s], t * 16 + 16)
                    b_all = b_in[:, s, :].rearrange("p (r f e) -> p r f e", r=1, e=E).to_broadcast([P, FIELDS, F, E])
                    for c in range(CHUNKS):
                        g, q = c // GROUP_CHUNKS, c % GROUP_CHUNKS
                        if q == 0:
                            dve.wait_ge(projected, n * GROUPS + (g + 1))
                        if not (first_trip and s == 0 and c < OUT_SLOTS):
                            dve.wait_ge(stored[c % OUT_SLOTS],
                                        16 * (n * (CHUNKS // OUT_SLOTS) + c // OUT_SLOTS))
                            if first_trip and s == 0 and c == OUT_SLOTS:
                                dve.wait_ge(first_field_stored, 16)
                        p_chunk = proj[g % PROJ_SLOTS][:, q * FIELDS * E:(q + 1) * FIELDS * E].rearrange(
                            "p (r f e) -> p r f e", f=1, e=E).to_broadcast([P, FIELDS, F, E])
                        o = products[:, c % OUT_SLOTS, :].rearrange("p (r f e) -> p r f e", f=F, e=E)
                        r0 = 0
                        if first_trip and s == 0 and c == 0:
                            r0 = 1
                            nc.vector.tensor_tensor(o[:, 0:r0], p_chunk[:, 0:r0], b_all[:, 0:r0],
                                                    ALU.mult).then_inc(first_field_multiplied, 1)
                        nc.vector.tensor_tensor(o[:, r0:FIELDS], p_chunk[:, r0:FIELDS], b_all[:, r0:FIELDS],
                                                ALU.mult).then_inc(multiplied, 1)

            trip(0, True)
            with dve.Fori(1, TRIPS) as t:
                trip(t, False)


_INS = ['r_inputs_A', 'r_inputs_B', 'L0_rec_W']


def kernel(**inputs):
    import numpy as _np
    import concourse.bacc as _bacc
    from concourse import mybir as _mybir
    from concourse.bass_utils import run_bass_kernel_spmd as _run

    nc = _bacc.Bacc("TRN2", target_bir_lowering=False, num_devices=1)
    arrays, args = {}, []
    for name in _INS:
        a = _np.ascontiguousarray(inputs[name])
        arrays[f"in_{name}_dram"] = a
        args.append(nc.dram_tensor(f"in_{name}_dram", a.shape, _mybir.dt.from_np(a.dtype), kind="ExternalInput").ap())
    batch, fields, width = inputs['r_inputs_A'].shape
    args.append(nc.dram_tensor("out_0_dram", (batch, fields * fields, width), _mybir.dt.float32,
                               kind="ExternalOutput").ap())
    bass_field_pair_products(nc, *args)
    r = _run(nc, [arrays], core_ids=[0])
    return r.results[0]["out_0_dram"]
```
